# Optimizing a Trainium2 kernel written in Bass

```python
import numpy as np
import jax
import jax.numpy as jnp

def _softmax(x, axis=-1):
    return jax.nn.softmax(x, axis=axis)

def _gelu(x):
    return jax.nn.gelu(x, approximate=True)

def _silu(x):
    return jax.nn.silu(x)

def _sigmoid(x):
    return jax.nn.sigmoid(x)

def _layernorm(x, axis=-1, eps=1e-05):
    m = jnp.mean(x, axis=axis, keepdims=True)
    v = jnp.var(x, axis=axis, keepdims=True)
    return (x - m) / jnp.sqrt(v + eps)

def _scatter_add(tgt, idx, src, axis=0):
    return tgt.at[idx].add(src)

def _segment_sum(src, seg, n):
    return jax.ops.segment_sum(src, seg, n)
kernel_name = 'mk_xattn_seq_d1_seqx_r2_879c67'

def setup_inputs(seed: int=0):
    np.random.seed(seed)
    _w = jnp.asarray

    def _rec_inputs():
        import jax
        import jax.numpy as jnp
        _rk = jax.random.key(seed)
        x = 7.22e-05 + 1 * jax.random.normal(jax.random.fold_in(_rk, 1), (32, 256, 1024), jnp.float32)
        _lenS = 256 - jax.random.randint(jax.random.fold_in(_rk, 7), (32,), 0, max(1, 256 // 4) + 1, jnp.int32)
        _lenS2 = 256 - jax.random.randint(jax.random.fold_in(_rk, 8), (32,), 0, max(1, 256 // 4) + 1, jnp.int32)
        _ctx_2048P = jax.random.normal(jax.random.fold_in(_rk, 11), (32, 16, 1024), jnp.float32)
        _ctx_2048c = jax.random.dirichlet(jax.random.fold_in(_rk, 511), 0.3 * jnp.ones((16,), jnp.float32), (32, 256))
        _ctx_2048t = jnp.einsum('bsk,bkd->bsd', _ctx_2048c, _ctx_2048P)
        _ctx_2048t = _ctx_2048t * jax.lax.rsqrt(jnp.mean(jnp.square(_ctx_2048t)) + 1e-12) * 0.953939
        ctx_2048 = 4.13588e-05 + 0.999923 * (_ctx_2048t + 0.3 * jax.random.normal(jax.random.fold_in(_rk, 611), (32, 256, 1024), jnp.float32))
        return (x, ctx_2048)
    x, ctx_2048 = _rec_inputs()

    def _L0_xattn_setup():
        import jax, jax.numpy as jnp
        import numpy as np
        B, C, N = (8, 256, 1024)
        key = jax.random.key(seed)
        ks = jax.random.split(key, 7)
        s = 1.0 / np.sqrt(C)
        return {'x': jax.random.normal(ks[0], (B, C, N), dtype=jnp.float32), 'y': jax.random.normal(ks[1], (B, C, N), dtype=jnp.float32), 'w_qk': jax.random.normal(ks[2], (C, C), dtype=jnp.float32) * s, 'w_v': jax.random.normal(ks[3], (C, C), dtype=jnp.float32) * s, 'b_v': jax.random.normal(ks[4], (C,), dtype=jnp.float32) * s, 'w_t': jax.random.normal(ks[5], (C, C), dtype=jnp.float32) * s, 'b_t': jax.random.normal(ks[6], (C,), dtype=jnp.float32) * s}
    _L0_xattn_all = _L0_xattn_setup()
    _L0_xattn_in = {k: v for k, v in _L0_xattn_all.items() if k in ('w_qk', 'w_v', 'b_v', 'w_t', 'b_t')}
    del _L0_xattn_all
    return {'x': x, 'ctx_2048': ctx_2048, 'L0_xattn_w_qk': _L0_xattn_in['w_qk'], 'L0_xattn_w_v': _L0_xattn_in['w_v'], 'L0_xattn_b_v': _L0_xattn_in['b_v'], 'L0_xattn_w_t': _L0_xattn_in['w_t'], 'L0_xattn_b_t': _L0_xattn_in['b_t']}

def reference(x, ctx_2048, L0_xattn_w_qk, L0_xattn_w_v, L0_xattn_b_v, L0_xattn_w_t, L0_xattn_b_t):
    import jax
    import jax.numpy as jnp

    def _L0_xattn_ref(x, y, w_qk, w_v, b_v, w_t, b_t):
        import jax, jax.numpy as jnp
        import numpy as np
        B, C, N = (8, 256, 1024)
        x_q = jnp.einsum('oc,bcn->bno', w_qk, y)
        x_k = jnp.einsum('oc,bcn->bon', w_qk, x)
        x_v = jnp.einsum('oc,bcn->bon', w_v, x) + b_v[None, :, None]
        energy = jnp.einsum('bnc,bcm->bnm', x_q, x_k)
        attention = jax.nn.softmax(energy, axis=-1)
        attention = attention / (1e-07 + attention.sum(axis=1, keepdims=True))
        x_r = jnp.einsum('bcn,bnm->bcm', x_v, attention)
        x_r = jax.nn.relu(jnp.einsum('oc,bcn->bon', w_t, x - x_r) + b_t[None, :, None])
        return x + x_r
    x = _L0_xattn_ref(x, ctx_2048, L0_xattn_w_qk, L0_xattn_w_v, L0_xattn_b_v, L0_xattn_w_t, L0_xattn_b_t)
    return x

_drawn_inputs = setup_inputs


def setup_inputs(seed=0):
    import zlib

    import numpy as np

    out = dict(_drawn_inputs(seed))
    spreads = {}
    factors = {}
    for name, (base, spread) in spreads.items():
        noise = np.random.default_rng([zlib.crc32(name.encode()), seed]).standard_normal(out[name].shape)
        drawn = base * np.exp(spread * noise) if base else spread * noise
        out[name] = jnp.asarray(drawn.astype(out[name].dtype))
    for name, factor in factors.items():
        out[name] = (out[name] * factor).astype(out[name].dtype)
    return out
```

```python
import concourse.bass as bass
from concourse import mybir
from contextlib import ExitStack

FP32 = mybir.dt.float32
FP32R = mybir.dt.float32r
ALU = mybir.AluOpType
ACT = mybir.ActivationFunctionType
AX = mybir.AxisListType

P = 128
BANK = 512
EPS = 1e-07


def xattn_kernel(nc: bass.Bass, x: bass.AP, y: bass.AP, w_qk: bass.AP, w_v: bass.AP, b_v: bass.AP,
                 w_t_T: bass.AP, b_t: bass.AP, out: bass.AP):
    B, C, N = x.shape
    KT = C // P
    NT = N // P
    NH = N // BANK
    HT = NT // 2
    HN = N // 2
    DMA = 16

    def by_channel(ap):
        return ap.rearrange("(k p) n -> p k n", p=P)

    x_dram = x.rearrange("b (k p) n -> b p k n", p=P)
    y_dram = y.rearrange("b (k p) n -> b p k n", p=P)
    out_dram = out.rearrange("b (k p) n -> b p k n", p=P)

    ctx = ExitStack()
    with ctx:
        def sb(name, shape, dt=FP32):
            return ctx.enter_context(nc.sbuf_tensor(name, shape, dt))

        def sem(name):
            return ctx.enter_context(nc.semaphore(name))

        wqk_sb = sb("wqk_sb", [P, KT, C])
        wv_sb = sb("wv_sb", [P, KT, C])
        wtT_sb = sb("wtT_sb", [P, KT, C])
        bv_sb = sb("bv_sb", [P, KT])
        bt_sb = sb("bt_sb", [P, KT])
        g_hi, g_lo = sb("g_hi", [P, KT, C], FP32R), sb("g_lo", [P, KT, C], FP32R)
        hnT = sb("hnT", [P, KT, C])
        hnT_hi, hnT_lo = sb("hnT_hi", [P, KT, C], FP32R), sb("hnT_lo", [P, KT, C], FP32R)
        wtT_hi, wtT_lo = sb("wtT_hi", [P, KT, C], FP32R), sb("wtT_lo", [P, KT, C], FP32R)
        bn_row = sb("bn_row", [P, C])
        ones_col = sb("ones_col", [P, 1])
        ident = sb("ident", [P, P])
        ident_r = sb("ident_r", [P, P], FP32R)
        x_sb = [sb(f"x_sb{i}", [P, KT, N]) for i in range(2)]
        x_hi = [sb(f"x_hi{i}", [P, KT, N], FP32R) for i in range(2)]
        x_lo = [sb(f"x_lo{i}", [P, KT, N], FP32R) for i in range(2)]
        gx_hi = [sb(f"gx_hi{i}", [P, KT, N], FP32R) for i in range(2)]
        gx_lo = [sb(f"gx_lo{i}", [P, KT, N], FP32R) for i in range(2)]
        y_sb = sb("y_sb", [P, KT, N])
        y_hi, y_lo = sb("y_hi", [P, KT, N], FP32R), sb("y_lo", [P, KT, N], FP32R)
        z_sb = sb("z_sb", [P, NT, C])
        wx_sb = sb("wx_sb", [P, KT, N])
        res = sb("res", [P, KT, N])
        colsum = [sb(f"colsum{i}", [P, N]) for i in range(2)]
        s_eps, s_inv = sb("s_eps", [P, NT]), sb("s_inv", [P, NT])
        s_inv_hi, s_inv_lo = sb("s_inv_hi", [P, NT], FP32R), sb("s_inv_lo", [P, NT], FP32R)
        neg_max = [sb(f"neg_max{i}", [P, NT]) for i in range(2)]
        row_sum = [sb(f"row_sum{i}", [P, NT]) for i in range(2)]
        row_inv = [sb(f"row_inv{i}", [P, NT]) for i in range(2)]
        p_sb = [sb(f"p_sb{i}", [P, N]) for i in range(2)]
        p_hi = [sb(f"p_hi{i}", [P, N], FP32R) for i in range(2)]
        p_lo = [sb(f"p_lo{i}", [P, N], FP32R) for i in range(2)]
        v_hi = [sb(f"v_hi{i}", [P, C], FP32R) for i in range(2)]
        v_lo = [sb(f"v_lo{i}", [P, C], FP32R) for i in range(2)]
        pv = ctx.enter_context(nc.psum_tensor("pv", [P, KT, N], FP32))
        slot = [ctx.enter_context(nc.psum_tensor(f"slot{i}", [P, N], FP32)) for i in range(2)]

        weights_in, x_in, y_in, out_stored = sem("weights_in"), sem("x_in"), sem("y_in"), sem("out_stored")
        ident_made = sem("ident_made")
        setup_mm, setup_dve = sem("setup_mm"), sem("setup_dve")
        e_done, pv_done, z_done = sem("e_done"), sem("pv_done"), sem("z_done")
        w_done, g_done = sem("w_done"), sem("g_done")
        cs_done, sb_done = sem("cs_done"), sem("sb_done")
        exp_done, p_hi_done, v_hi_done = sem("exp_done"), sem("p_hi_done"), sem("v_hi_done")
        x_hi_done, y_hi_done, gx_hi_done = sem("x_hi_done"), sem("y_hi_done"), sem("gx_hi_done")
        pv_copied, wx_done = sem("pv_copied"), sem("wx_done")
        max_done, z_copied, inv_done = sem("max_done"), sem("z_copied"), sem("inv_done")
        p_lo_done, v_lo_done, acc_done = sem("p_lo_done"), sem("v_lo_done"), sem("acc_done")
        gx_lo_done, s_read, s_step, s_ready = sem("gx_lo_done"), sem("s_read"), sem("s_step"), sem("s_ready")
        scaled, out_ready = sem("scaled"), sem("out_ready")
        x_lo_done, y_lo_done, wx_added = sem("x_lo_done"), sem("y_lo_done"), sem("wx_added")

        block = ctx.enter_context(nc.Block())

        def run_batches(eng, first, middle, last):
            first(0)
            with eng.Fori(0, (B - 2) // 2) as i:
                middle(2 * i + 1, 1)
                middle(2 * i + 2, 0)
            last(B - 1)

        @block.sync
        def _(sp):
            def load_x(b, par):
                sp.dma_start(x_sb[par][:, :, :], x_dram[b]).then_inc(x_in, DMA)

            def load_y(b):
                sp.dma_start(y_sb[:, :, :], y_dram[b]).then_inc(y_in, DMA)

            def store(b):
                sp.wait_ge(out_ready, b + 1)
                sp.dma_start(out_dram[b], res[:, :, :]).then_inc(out_stored, DMA)

            def batch(b, par, first=False, last=False):
                if not last:
                    sp.wait_ge(y_hi_done, 2 * b + 2)
                    sp.wait_ge(y_lo_done, 2 * b + 2)
                    load_y(b + 1)
                if not first:
                    store(b - 1)
                if not last:
                    load_x(b + 1, 1 - par)

            sp.dma_start(wqk_sb[:, :, :], by_channel(w_qk)).then_inc(weights_in, DMA)
            load_x(0, 0)
            sp.dma_start(wtT_sb[:, :, :], by_channel(w_t_T)).then_inc(weights_in, DMA)
            sp.dma_start(wv_sb[:, :, :], by_channel(w_v)).then_inc(weights_in, DMA)
            with nc.allow_non_contiguous_dma(reason="256 biases, once"):
                sp.dma_start(bv_sb[:, :], b_v.rearrange("(k p) -> p k", p=P)).then_inc(weights_in, DMA)
                sp.dma_start(bt_sb[:, :], b_t.rearrange("(k p) -> p k", p=P)).then_inc(weights_in, DMA)
            load_y(0)
            run_batches(sp, lambda b: batch(b, 0, first=True), batch, lambda b: batch(b, 1, last=True))
            store(B - 1)
            sp.wait_ge(out_stored, DMA * B)

        @block.gpsimd
        def _(pool):
            def x_low(b, par):
                pool.wait_ge(x_hi_done, b + 1)
                nc.gpsimd.tensor_tensor(x_lo[par][:, :, :], x_sb[par][:, :, :],
                                        x_hi[par][:, :, :].bitcast(FP32), ALU.subtract).then_inc(x_lo_done, 1)

            def y_low(b, half):
                cols = slice(half * HN, (half + 1) * HN)
                pool.wait_ge(y_hi_done, 2 * b + half + 1)
                nc.gpsimd.tensor_tensor(y_lo[:, :, cols], y_sb[:, :, cols],
                                        y_hi[:, :, cols].bitcast(FP32), ALU.subtract).then_inc(y_lo_done, 1)

            def add_wx(b):
                pool.wait_ge(scaled, b + 1)
                pool.wait_ge(wx_done, 2 * b + 2)
                nc.gpsimd.tensor_tensor(res[:, :, :], res[:, :, :], wx_sb[:, :, :], ALU.add).then_inc(wx_added, 1)

            def batch(b, par, first=False, last=False):
                y_low(b, 1)
                if not first:
                    add_wx(b - 1)
                if not last:
                    y_low(b + 1, 0)
                    x_low(b + 1, 1 - par)

            nc.gpsimd.memset(ones_col[:, :], 1.0)
            nc.gpsimd.memset(ident[:, :], 0.0).then_inc(ident_made, 1)
            pool.wait_ge(ident_made, 1)
            nc.gpsimd.affine_select(out=ident[:, :], in_=ident[:, :], compare_op=ALU.not_equal, fill=1.0,
                                    base=0, pattern=[[-1, P]], channel_multiplier=1).then_inc(ident_made, 1)
            x_low(0, 0)
            y_low(0, 0)
            run_batches(pool, lambda b: batch(b, 0, first=True), batch, lambda b: batch(b, 1, last=True))
            add_wx(B - 1)

        @block.scalar
        def _(act):
            def x_high(b, par):
                act.wait_ge(x_in, DMA * (b + 1))
                nc.scalar.activation(x_hi[par][:, :, :], x_sb[par][:, :, :], ACT.Copy).then_inc(x_hi_done, 1)

            def y_high(b, half, first=False):
                cols = slice(half * HN, (half + 1) * HN)
                act.wait_ge(y_in, DMA * (b + 1))
                if not first:
                    act.wait_ge(e_done, NT * (b - 1) + HT * (half + 1))
                nc.scalar.activation(y_hi[:, :, cols], y_sb[:, :, cols], ACT.Copy).then_inc(y_hi_done, 1)

            def gx_high(b, par, mt, s):
                act.wait_ge(g_done, KT * b + mt + 1)
                nc.scalar.activation(gx_hi[par][:, mt, :], slot[s][:, :], ACT.Copy).then_inc(gx_hi_done, 1)

            def exponent(b, par, j, s):
                act.wait_ge(max_done, NT * b + j + 1)
                if j >= 2 or not isinstance(b, int) or b > 0:
                    act.wait_ge(acc_done, NT * b + j - 1)
                nc.scalar.activation(p_sb[j % 2][:, :], slot[s][:, :], ACT.Exp, bias=neg_max[par][:, j:j + 1],
                                     accum_out=row_sum[par][:, j:j + 1]).then_inc(exp_done, 1)

            def p_high(b, j):
                act.wait_ge(exp_done, NT * b + j + 1)
                if j >= 2 or not isinstance(b, int) or b > 0:
                    act.wait_ge(pv_done, NT * b + j - 1)
                nc.scalar.activation(p_hi[j % 2][:, :], p_sb[j % 2][:, :], ACT.Copy).then_inc(p_hi_done, 1)

            def v_high(b, par, j):
                act.wait_ge(z_copied, 2 * b + j // HT + 1)
                act.wait_ge(inv_done, NT * b + j + 1)
                nc.scalar.activation(v_hi[j % 2][:, :], z_sb[:, j, :], ACT.Copy,
                                     scale=row_inv[par][:, j:j + 1]).then_inc(v_hi_done, 1)

            def tile(b, par, j, s):
                exponent(b, par, j, s)
                p_high(b, j)
                v_high(b, par, j)

            def copy_pv(b, first=False):
                act.wait_ge(pv_done, NT * (b + 1))
                if not first:
                    act.wait_ge(out_stored, DMA * b)
                nc.scalar.activation(res[:, :, :], pv[:, :, :], ACT.Copy).then_inc(pv_copied, 1)

            def wx(b, mt, s, first=False):
                act.wait_ge(w_done, KT * b + mt + 1)
                if not first:
                    act.wait_ge(wx_added, b)
                nc.scalar.activation(wx_sb[:, mt, :], slot[s][:, :], ACT.Identity,
                                     bias=bt_sb[:, mt:mt + 1]).then_inc(wx_done, 1)

            def batch(b, par, first=False, second=False, last=False):
                tile(b, par, 0, 0)
                y_high(b, 1, first=first)
                if not first:
                    copy_pv(b - 1, first=second)
                tile(b, par, 1, 1)
                tile(b, par, 2, 0)
                tile(b, par, 3, 1)
                wx(b, 0, 0, first=first)
                tile(b, par, 4, 1)
                wx(b, 1, 0, first=first)
                if not last:
                    y_high(b + 1, 0)
                tile(b, par, 5, 1)
                if not last:
                    x_high(b + 1, 1 - par)
                exponent(b, par, 6, 0)
                p_high(b, 6)
                if not last:
                    gx_high(b + 1, 1 - par, 0, 1)
                v_high(b, par, 6)
                if not last:
                    gx_high(b + 1, 1 - par, 1, 0)
                tile(b, par, 7, 1)

            x_high(0, 0)
            y_high(0, 0, first=True)
            gx_high(0, 0, 0, 1)
            gx_high(0, 0, 1, 0)
            act.wait_ge(weights_in, 5 * DMA)
            batch(0, 0, first=True)
            batch(1, 1, second=True)
            with act.Fori(0, (B - 4) // 2) as i:
                batch(2 * i + 2, 0)
                batch(2 * i + 3, 1)
            batch(B - 2, 0)
            batch(B - 1, 1, last=True)
            copy_pv(B - 1)

        @block.vector
        def _(dve):
            setup_steps = [0]

            def setup(ins):
                setup_steps[0] += 1
                ins.then_inc(setup_dve, 1)
                dve.wait_ge(setup_dve, setup_steps[0])

            def gx_low(b, par, mt, s):
                dve.wait_ge(gx_hi_done, KT * b + mt + 1)
                nc.vector.tensor_tensor(gx_lo[par][:, mt, :], slot[s][:, :],
                                        gx_hi[par][:, mt, :].bitcast(FP32), ALU.subtract).then_inc(gx_lo_done, 1)

            def row_max(b, par, j, s):
                dve.wait_ge(e_done, NT * b + j + 1)
                nc.vector.tensor_reduce(neg_max[par][:, j:j + 1], slot[s][:, :], AX.X, ALU.max,
                                        negate=True).then_inc(max_done, 1)

            def z_copy(b, half, s):
                dve.wait_ge(z_done, 2 * b + half + 1)
                bias = bn_row[:, :].rearrange("p (a o) -> p a o", a=1).to_broadcast([P, HT, C])
                nc.vector.tensor_tensor(z_sb[:, half * HT:(half + 1) * HT, :],
                                        slot[s][:, :].rearrange("p (t o) -> p t o", t=HT), bias,
                                        ALU.add).then_inc(z_copied, 1)

            def rest(b, par, j):
                t = j % 2
                inv = row_inv[par][:, j:j + 1]
                dve.wait_ge(exp_done, NT * b + j + 1)
                nc.vector.reciprocal(inv, row_sum[par][:, j:j + 1]).then_inc(inv_done, 1)
                dve.wait_ge(p_hi_done, NT * b + j + 1)
                nc.vector.tensor_tensor(p_lo[t][:, :], p_sb[t][:, :], p_hi[t][:, :].bitcast(FP32),
                                        ALU.subtract).then_inc(p_lo_done, 1)
                dve.wait_ge(inv_done, NT * b + j + 1)
                if j == 0:
                    nc.vector.tensor_scalar(colsum[par][:, :], p_sb[t][:, :], inv, None,
                                            ALU.mult).then_inc(acc_done, 1)
                else:
                    dve.wait_ge(acc_done, NT * b + j)
                    nc.vector.scalar_tensor_tensor(out=colsum[par][:, :], in0=p_sb[t][:, :], scalar=inv,
                                                   in1=colsum[par][:, :], op0=ALU.mult,
                                                   op1=ALU.add).then_inc(acc_done, 1)
                dve.wait_ge(v_hi_done, NT * b + j + 1)
                nc.vector.scalar_tensor_tensor(out=v_lo[t][:, :], in0=z_sb[:, j, :], scalar=inv,
                                               in1=v_hi[t][:, :].bitcast(FP32), op0=ALU.mult,
                                               op1=ALU.subtract).then_inc(v_lo_done, 1)

            def col_inverse(b, s):
                dve.wait_ge(cs_done, b + 1)
                nc.vector.tensor_scalar(s_eps[:, :], slot[s][:, 0:NT], EPS, None, ALU.add).then_inc(s_read, 1)
                dve.wait_ge(s_read, b + 1)
                nc.vector.reciprocal(s_inv[:, :], s_eps[:, :]).then_inc(s_step, 1)
                dve.wait_ge(s_step, 2 * b + 1)
                nc.vector.tensor_copy(s_inv_hi[:, :], s_inv[:, :]).then_inc(s_step, 1)
                dve.wait_ge(s_step, 2 * b + 2)
                nc.vector.tensor_tensor(s_inv_lo[:, :], s_inv[:, :], s_inv_hi[:, :].bitcast(FP32),
                                        ALU.subtract).then_inc(s_ready, 1)

            def scale(b, s):
                dve.wait_ge(pv_copied, b + 1)
                dve.wait_ge(sb_done, b + 1)
                inv = slot[s][:, :].rearrange("p (a n) -> p a n", a=1).to_broadcast([P, KT, N])
                nc.vector.tensor_tensor(res[:, :, :], res[:, :, :], inv, ALU.mult).then_inc(scaled, 1)

            def finish(b, par):
                dve.wait_ge(wx_added, b + 1)
                nc.vector.scalar_tensor_tensor(out=res[:, :, :], in0=res[:, :, :], scalar=0.0,
                                               in1=x_sb[par][:, :, :], op0=ALU.max,
                                               op1=ALU.add).then_inc(out_ready, 1)

            def batch(b, par, first=False, last=False):
                row_max(b, par, 0, 0)
                z_copy(b, 0, 1)
                rest(b, par, 0)
                if not first:
                    col_inverse(b - 1, 0)
                row_max(b, par, 1, 1)
                z_copy(b, 1, 0)
                rest(b, par, 1)
                row_max(b, par, 2, 0)
                if not first:
                    scale(b - 1, 1)
                rest(b, par, 2)
                row_max(b, par, 3, 1)
                rest(b, par, 3)
                row_max(b, par, 4, 1)
                if not first:
                    finish(b - 1, 1 - par)
                rest(b, par, 4)
                row_max(b, par, 5, 1)
                rest(b, par, 5)
                row_max(b, par, 6, 0)
                if not last:
                    gx_low(b + 1, 1 - par, 0, 1)
                rest(b, par, 6)
                if not last:
                    gx_low(b + 1, 1 - par, 1, 0)
                row_max(b, par, 7, 1)
                rest(b, par, 7)

            dve.wait_ge(setup_mm, 1)
            g_ps = slot[0][:, 0:KT * C].rearrange("p (k c) -> p k c", k=KT)
            setup(nc.vector.tensor_copy(g_hi[:, :, :], g_ps))
            setup(nc.vector.tensor_tensor(g_lo[:, :, :], g_ps, g_hi[:, :, :].bitcast(FP32), ALU.subtract))
            dve.wait_ge(weights_in, 5 * DMA)
            setup(nc.vector.tensor_copy(wtT_hi[:, :, :], wtT_sb[:, :, :]))
            setup(nc.vector.tensor_tensor(wtT_lo[:, :, :], wtT_sb[:, :, :], wtT_hi[:, :, :].bitcast(FP32),
                                          ALU.subtract))
            dve.wait_ge(setup_mm, 2)
            h_ps = slot[1][:, 0:KT * C].rearrange("p (k c) -> p k c", k=KT)
            setup(nc.vector.tensor_scalar(hnT[:, :, :], h_ps, -1.0, None, ALU.mult))
            setup(nc.vector.tensor_scalar(bn_row[:, :], slot[1][:, BANK:BANK + C], -1.0, None, ALU.mult))
            setup(nc.vector.tensor_copy(hnT_hi[:, :, :], hnT[:, :, :]))
            setup(nc.vector.tensor_tensor(hnT_lo[:, :, :], hnT[:, :, :], hnT_hi[:, :, :].bitcast(FP32),
                                          ALU.subtract))
            dve.wait_ge(ident_made, 2)
            setup(nc.vector.tensor_copy(ident_r[:, :], ident[:, :]))
            gx_low(0, 0, 0, 1)
            gx_low(0, 0, 1, 0)
            run_batches(dve, lambda b: batch(b, 0, first=True), batch, lambda b: batch(b, 1, last=True))
            col_inverse(B - 1, 0)
            scale(B - 1, 1)
            finish(B - 1, 1)

        @block.tensor
        def _(pe):
            def three_passes(a_hi, a_lo, b_hi, b_lo):
                return ((a_hi, b_hi), (a_hi, b_lo), (a_lo, b_hi))

            def rows_by_n(s, lhs_hi, lhs_lo, lhs_cols, rhs_hi, rhs_lo):
                for kt in range(KT):
                    for n, (a, b) in enumerate(three_passes(lhs_hi, lhs_lo, rhs_hi, rhs_lo)):
                        for nh in range(NH):
                            cols = slice(nh * BANK, (nh + 1) * BANK)
                            last = nc.tensor.matmul(slot[s][:, cols], a[:, kt, lhs_cols], b[:, kt, cols],
                                                    start=(kt == 0 and n == 0), stop=(kt == KT - 1 and n == 2))
                return last

            def rows_of(tile):
                return slice(tile * P, (tile + 1) * P)

            def energy(b, par, j, s):
                rows_by_n(s, y_hi, y_lo, rows_of(j), gx_hi[par], gx_lo[par]).then_inc(e_done, 1)

            def z_part(b, par, half, s):
                for t in range(HT):
                    cols = slice(t * C, (t + 1) * C)
                    for kt in range(KT):
                        for n, (a, h) in enumerate(three_passes(x_hi[par], x_lo[par], hnT_hi, hnT_lo)):
                            last = nc.tensor.matmul(slot[s][:, cols], a[:, kt, rows_of(half * HT + t)], h[:, kt, :],
                                                    start=(kt == 0 and n == 0), stop=(kt == KT - 1 and n == 2))
                last.then_inc(z_done, 1)

            def w_part(b, par, mt, s):
                rows_by_n(s, wtT_hi, wtT_lo, rows_of(mt), x_hi[par], x_lo[par]).then_inc(w_done, 1)

            def g_part(b, par, mt, s):
                rows_by_n(s, g_hi, g_lo, rows_of(mt), x_hi[par], x_lo[par]).then_inc(g_done, 1)

            def pv_tile(b, j):
                pe.wait_ge(p_lo_done, NT * b + j + 1)
                pe.wait_ge(v_lo_done, NT * b + j + 1)
                t = j % 2
                for mt in range(KT):
                    for n, (v, p) in enumerate(three_passes(v_hi[t], v_lo[t], p_hi[t], p_lo[t])):
                        for nh in range(NH):
                            cols = slice(nh * BANK, (nh + 1) * BANK)
                            last = nc.tensor.matmul(pv[:, mt, cols], v[:, rows_of(mt)], p[:, cols],
                                                    start=(j == 0 and n == 0), stop=(j == NT - 1 and n == 2))
                last.then_inc(pv_done, 1)

            def column_sum(b, par, s):
                pe.wait_ge(acc_done, NT * (b + 1))
                for mt in range(NT):
                    last = nc.tensor.matmul(slot[s][:, mt:mt + 1], colsum[par][:, rows_of(mt)], ones_col[:, :],
                                            start=True, stop=True)
                last.then_inc(cs_done, 1)

            def spread(b, s):
                pe.wait_ge(s_ready, b + 1)
                for mt in range(NT):
                    for n, part in enumerate((s_inv_hi, s_inv_lo)):
                        last = nc.tensor.matmul(slot[s][:, rows_of(mt)], part[:, mt:mt + 1].to_broadcast([P, P]),
                                                ident_r[:, :], start=(n == 0), stop=(n == 1))
                last.then_inc(sb_done, 1)

            def batch(b, par, first=False, last=False):
                pe.wait_ge(gx_lo_done, KT * (b + 1))
                pe.wait_ge(y_lo_done, 2 * b + 1)
                energy(b, par, 0, 0)
                if not first:
                    pe.wait_ge(exp_done, NT * b)
                z_part(b, par, 0, 1)
                if not first:
                    pv_tile(b - 1, NT - 1)
                pe.wait_ge(exp_done, NT * b + 1)
                if not first:
                    column_sum(b - 1, 1 - par, 0)
                pe.wait_ge(z_copied, 2 * b + 1)
                energy(b, par, 1, 1)
                if not first:
                    pe.wait_ge(s_read, b)
                z_part(b, par, 1, 0)
                if not first:
                    pe.wait_ge(pv_copied, b)
                pv_tile(b, 0)
                pe.wait_ge(exp_done, NT * b + 2)
                if not first:
                    spread(b - 1, 1)
                pe.wait_ge(z_copied, 2 * b + 2)
                energy(b, par, 2, 0)
                pv_tile(b, 1)
                if not first:
                    pe.wait_ge(scaled, b)
                energy(b, par, 3, 1)
                pe.wait_ge(exp_done, NT * b + 3)
                w_part(b, par, 0, 0)
                pv_tile(b, 2)
                pe.wait_ge(exp_done, NT * b + 4)
                pe.wait_ge(y_lo_done, 2 * b + 2)
                energy(b, par, 4, 1)
                pe.wait_ge(wx_done, KT * b + 1)
                w_part(b, par, 1, 0)
                pv_tile(b, 3)
                pe.wait_ge(exp_done, NT * b + 5)
                energy(b, par, 5, 1)
                pv_tile(b, 4)
                pe.wait_ge(wx_done, KT * b + 2)
                energy(b, par, 6, 0)
                pe.wait_ge(exp_done, NT * b + 6)
                if not last:
                    pe.wait_ge(x_lo_done, b + 2)
                    g_part(b + 1, 1 - par, 0, 1)
                pv_tile(b, 5)
                if not last:
                    pe.wait_ge(exp_done, NT * b + 7)
                    g_part(b + 1, 1 - par, 1, 0)
                    pe.wait_ge(gx_lo_done, KT * (b + 1) + 1)
                energy(b, par, 7, 1)
                pv_tile(b, 6)

            pe.wait_ge(weights_in, 5 * DMA)
            for ct in range(KT):
                for kt in range(KT):
                    last = nc.tensor.matmul(slot[0][:, ct * C:(ct + 1) * C], wqk_sb[:, kt, rows_of(ct)],
                                            wqk_sb[:, kt, :], start=(kt == 0), stop=(kt == KT - 1))
            last.then_inc(setup_mm, 1)
            for ct in range(KT):
                for kt in range(KT):
                    nc.tensor.matmul(slot[1][:, ct * C:(ct + 1) * C], wv_sb[:, kt, rows_of(ct)], wtT_sb[:, kt, :],
                                     start=(kt == 0), stop=(kt == KT - 1))
            for kt in range(KT):
                last = nc.tensor.matmul(slot[1][:, BANK:BANK + C], bv_sb[:, kt:kt + 1].to_broadcast([P, P]),
                                        wtT_sb[:, kt, :], start=(kt == 0), stop=(kt == KT - 1))
            last.then_inc(setup_mm, 1)
            pe.wait_ge(setup_dve, 9)
            pe.wait_ge(x_lo_done, 1)
            g_part(0, 0, 0, 1)
            g_part(0, 0, 1, 0)
            run_batches(pe, lambda b: batch(b, 0, first=True), batch, lambda b: batch(b, 1, last=True))
            pv_tile(B - 1, NT - 1)
            column_sum(B - 1, 1, 0)
            pe.wait_ge(exp_done, NT * B)
            spread(B - 1, 1)


def kernel(x, ctx_2048, L0_xattn_w_qk, L0_xattn_w_v, L0_xattn_b_v, L0_xattn_w_t, L0_xattn_b_t):
    import numpy as np
    import concourse.bacc as bacc
    from concourse.bass_utils import run_bass_kernel_spmd

    nc = bacc.Bacc("TRN2", target_bir_lowering=False, num_devices=1)
    given = {
        "x": x, "y": ctx_2048, "w_qk": L0_xattn_w_qk, "w_v": L0_xattn_w_v, "b_v": L0_xattn_b_v,
        "w_t_T": np.asarray(L0_xattn_w_t).T, "b_t": L0_xattn_b_t,
    }
    arrays, aps = {}, []
    for name, value in given.items():
        a = np.ascontiguousarray(value)
        arrays[name] = a
        aps.append(nc.dram_tensor(name, a.shape, mybir.dt.from_np(a.dtype), kind="ExternalInput").ap())
    aps.append(nc.dram_tensor("out", arrays["x"].shape, FP32, kind="ExternalOutput").ap())
    xattn_kernel(nc, *aps)
    result = run_bass_kernel_spmd(nc, [arrays], core_ids=[0])
    return result.results[0]["out"]
```

```python
import concourse.bass as bass
from concourse import mybir
from contextlib import ExitStack

FP32 = mybir.dt.float32
FP32R = mybir.dt.float32r
ALU = mybir.AluOpType
ACT = mybir.ActivationFunctionType
AX = mybir.AxisListType

P = 128
BANK = 512
EPS = 1e-07


def xattn_kernel(nc: bass.Bass, x: bass.AP, y: bass.AP, w_qk: bass.AP, w_v: bass.AP, b_v: bass.AP,
                 w_t_T: bass.AP, b_t: bass.AP, out: bass.AP):
    B, C, N = x.shape
    KT = C // P
    NT = N // P
    NH = N // BANK
    HT = NT // 2
    HN = N // 2
    DMA = 16

    def by_channel(ap):
        return ap.rearrange("(k p) n -> p k n", p=P)

    x_dram = x.rearrange("b (k p) n -> b p k n", p=P)
    y_dram = y.rearrange("b (k p) n -> b p k n", p=P)
    out_dram = out.rearrange("b (k p) n -> b p k n", p=P)

    ctx = ExitStack()
    with ctx:
        def sb(name, shape, dt=FP32):
            return ctx.enter_context(nc.sbuf_tensor(name, shape, dt))

        def sem(name):
            return ctx.enter_context(nc.semaphore(name))

        wqk_sb = sb("wqk_sb", [P, KT, C])
        wv_sb = sb("wv_sb", [P, KT, C])
        wtT_sb = sb("wtT_sb", [P, KT, C])
        bv_sb = sb("bv_sb", [P, KT])
        bt_sb = sb("bt_sb", [P, KT])
        g_hi, g_lo = sb("g_hi", [P, KT, C], FP32R), sb("g_lo", [P, KT, C], FP32R)
        hnT = sb("hnT", [P, KT, C])
        hnT_hi, hnT_lo = sb("hnT_hi", [P, KT, C], FP32R), sb("hnT_lo", [P, KT, C], FP32R)
        wtT_hi, wtT_lo = sb("wtT_hi", [P, KT, C], FP32R), sb("wtT_lo", [P, KT, C], FP32R)
        bn_row = sb("bn_row", [P, C])
        ident = sb("ident", [P, P])
        x_sb = [sb(f"x_sb{i}", [P, KT, N]) for i in range(2)]
        x_hi = [sb(f"x_hi{i}", [P, KT, N], FP32R) for i in range(2)]
        x_lo = [sb(f"x_lo{i}", [P, KT, N], FP32R) for i in range(2)]
        gx_hi = [sb(f"gx_hi{i}", [P, KT, N], FP32R) for i in range(2)]
        gx_lo = [sb(f"gx_lo{i}", [P, KT, N], FP32R) for i in range(2)]
        y_sb = sb("y_sb", [P, KT, N])
        y_hi, y_lo = sb("y_hi", [P, KT, N], FP32R), sb("y_lo", [P, KT, N], FP32R)
        z_sb = sb("z_sb", [P, NT, C])
        wx_sb = sb("wx_sb", [P, KT, N])
        res = sb("res", [P, KT, N])
        colsum = [sb(f"colsum{i}", [P, N]) for i in range(2)]
        s_sb, s_eps, s_inv = sb("s_sb", [P, NT]), sb("s_eps", [P, NT]), sb("s_inv", [P, NT])
        neg_max = [sb(f"neg_max{i}", [P, NT]) for i in range(2)]
        row_sum = [sb(f"row_sum{i}", [P, NT]) for i in range(2)]
        row_inv = [sb(f"row_inv{i}", [P, NT]) for i in range(2)]
        p_sb = [sb(f"p_sb{i}", [P, N]) for i in range(2)]
        p_hi = [sb(f"p_hi{i}", [P, N], FP32R) for i in range(2)]
        p_lo = [sb(f"p_lo{i}", [P, N], FP32R) for i in range(2)]
        v_hi = [sb(f"v_hi{i}", [P, C], FP32R) for i in range(2)]
        v_lo = [sb(f"v_lo{i}", [P, C], FP32R) for i in range(2)]
        pv = ctx.enter_context(nc.psum_tensor("pv", [P, KT, N], FP32))
        slot = [ctx.enter_context(nc.psum_tensor(f"slot{i}", [P, N], FP32)) for i in range(2)]

        wqk_in, weights_in, y_in = sem("wqk_in"), sem("weights_in"), sem("y_in")
        x_in = [sem(f"x_in{kt}") for kt in range(KT)]
        out_stored = [sem(f"out_stored{mt}") for mt in range(KT)]
        ident_made = sem("ident_made")
        setup_mm, setup_dve = sem("setup_mm"), sem("setup_dve")
        e_done, pv_done, z_done = sem("e_done"), sem("pv_done"), sem("z_done")
        w_done, g_done = sem("w_done"), sem("g_done")
        cs_done, sb_done = sem("cs_done"), sem("sb_done")
        exp_done, p_hi_done, v_hi_done = sem("exp_done"), sem("p_hi_done"), sem("v_hi_done")
        x_hi_done, y_hi_done, gx_hi_done = sem("x_hi_done"), sem("y_hi_done"), sem("gx_hi_done")
        pv_copied, wx_done = sem("pv_copied"), sem("wx_done")
        max_done, z_copied, inv_done = sem("max_done"), sem("z_copied"), sem("inv_done")
        p_lo_done, v_lo_done, acc_done = sem("p_lo_done"), sem("v_lo_done"), sem("acc_done")
        gx_lo_done, s_read, s_guarded, s_ready = sem("gx_lo_done"), sem("s_read"), sem("s_guarded"), sem("s_ready")
        scaled, out_ready = sem("scaled"), sem("out_ready")
        x_lo_done, y_lo_done, wx_added = sem("x_lo_done"), sem("y_lo_done"), sem("wx_added")

        block = ctx.enter_context(nc.Block())

        def run_batches(eng, first, middle, last):
            first(0)
            with eng.Fori(0, (B - 2) // 2) as i:
                middle(2 * i + 1, 1)
                middle(2 * i + 2, 0)
            last(B - 1)

        @block.sync
        def _(sp):
            def load_x(b, par, kt):
                sp.dma_start(x_sb[par][:, kt, :], x_dram[b][:, kt, :]).then_inc(x_in[kt], DMA)

            def load_y(b):
                sp.dma_start(y_sb[:, :, :], y_dram[b]).then_inc(y_in, DMA)

            def store(b, mt):
                sp.wait_ge(out_ready, KT * b + mt + 1)
                sp.dma_start(out_dram[b][:, mt, :], res[:, mt, :]).then_inc(out_stored[mt], DMA)

            def batch(b, par, first=False, last=False):
                if not last:
                    sp.wait_ge(y_hi_done, 2 * b + 2)
                    sp.wait_ge(y_lo_done, 2 * b + 2)
                    load_y(b + 1)
                for t in range(KT):
                    if not first:
                        store(b - 1, t)
                    if not last:
                        load_x(b + 1, 1 - par, t)

            sp.dma_start(wqk_sb[:, :, :], by_channel(w_qk)).then_inc(wqk_in, DMA)
            for kt in range(KT):
                load_x(0, 0, kt)
            load_y(0)
            sp.dma_start(wtT_sb[:, :, :], by_channel(w_t_T)).then_inc(weights_in, DMA)
            sp.dma_start(wv_sb[:, :, :], by_channel(w_v)).then_inc(weights_in, DMA)
            with nc.allow_non_contiguous_dma(reason="256 biases, once"):
                sp.dma_start(bv_sb[:, :], b_v.rearrange("(k p) -> p k", p=P)).then_inc(weights_in, DMA)
                sp.dma_start(bt_sb[:, :], b_t.rearrange("(k p) -> p k", p=P)).then_inc(weights_in, DMA)
            run_batches(sp, lambda b: batch(b, 0, first=True), batch, lambda b: batch(b, 1, last=True))
            for mt in range(KT):
                store(B - 1, mt)
            for mt in range(KT):
                sp.wait_ge(out_stored[mt], DMA * B)

        @block.gpsimd
        def _(pool):
            def x_low(b, par):
                for kt in range(KT):
                    pool.wait_ge(x_hi_done, KT * b + kt + 1)
                    nc.gpsimd.tensor_tensor(x_lo[par][:, kt, :], x_sb[par][:, kt, :],
                                            x_hi[par][:, kt, :].bitcast(FP32), ALU.subtract).then_inc(x_lo_done, 1)

            def y_low(b, half):
                cols = slice(half * HN, (half + 1) * HN)
                pool.wait_ge(y_hi_done, 2 * b + half + 1)
                nc.gpsimd.tensor_tensor(y_lo[:, :, cols], y_sb[:, :, cols],
                                        y_hi[:, :, cols].bitcast(FP32), ALU.subtract).then_inc(y_lo_done, 1)

            def add_wx(b):
                for mt in range(KT):
                    pool.wait_ge(scaled, KT * b + mt + 1)
                    pool.wait_ge(wx_done, KT * b + mt + 1)
                    nc.gpsimd.tensor_tensor(res[:, mt, :], res[:, mt, :], wx_sb[:, mt, :],
                                            ALU.add).then_inc(wx_added, 1)

            def batch(b, par, first=False, last=False):
                y_low(b, 1)
                if not first:
                    add_wx(b - 1)
                if not last:
                    x_low(b + 1, 1 - par)
                    y_low(b + 1, 0)

            nc.gpsimd.memset(ident[:, :], 0.0).then_inc(ident_made, 1)
            pool.wait_ge(ident_made, 1)
            nc.gpsimd.affine_select(out=ident[:, :], in_=ident[:, :], compare_op=ALU.not_equal, fill=1.0,
                                    base=0, pattern=[[-1, P]], channel_multiplier=1).then_inc(ident_made, 1)
            x_low(0, 0)
            y_low(0, 0)
            run_batches(pool, lambda b: batch(b, 0, first=True), batch, lambda b: batch(b, 1, last=True))
            add_wx(B - 1)

        @block.scalar
        def _(act):
            def x_high(b, par):
                for kt in range(KT):
                    act.wait_ge(x_in[kt], DMA * (b + 1))
                    nc.scalar.activation(x_hi[par][:, kt, :], x_sb[par][:, kt, :], ACT.Copy).then_inc(x_hi_done, 1)

            def y_high(b, half, first=False):
                cols = slice(half * HN, (half + 1) * HN)
                act.wait_ge(y_in, DMA * (b + 1))
                if not first:
                    act.wait_ge(e_done, NT * (b - 1) + HT * (half + 1))
                nc.scalar.activation(y_hi[:, :, cols], y_sb[:, :, cols], ACT.Copy).then_inc(y_hi_done, 1)

            def gx_high(b, par, mt, s):
                act.wait_ge(g_done, KT * b + mt + 1)
                nc.scalar.activation(gx_hi[par][:, mt, :], slot[s][:, :], ACT.Copy).then_inc(gx_hi_done, 1)

            def exponent(b, par, j, s):
                act.wait_ge(max_done, NT * b + j + 1)
                if j >= 2 or not isinstance(b, int) or b > 0:
                    act.wait_ge(acc_done, NT * b + j - 1)
                nc.scalar.activation(p_sb[j % 2][:, :], slot[s][:, :], ACT.Exp, bias=neg_max[par][:, j:j + 1],
                                     accum_out=row_sum[par][:, j:j + 1]).then_inc(exp_done, 1)

            def p_high(b, j):
                act.wait_ge(exp_done, NT * b + j + 1)
                if j >= 2 or not isinstance(b, int) or b > 0:
                    act.wait_ge(pv_done, NT * b + j - 1)
                nc.scalar.activation(p_hi[j % 2][:, :], p_sb[j % 2][:, :], ACT.Copy).then_inc(p_hi_done, 1)

            def v_high(b, par, j):
                act.wait_ge(z_copied, 2 * b + j // HT + 1)
                act.wait_ge(inv_done, NT * b + j + 1)
                nc.scalar.activation(v_hi[j % 2][:, :], z_sb[:, j, :], ACT.Copy,
                                     scale=row_inv[par][:, j:j + 1]).then_inc(v_hi_done, 1)

            def tile(b, par, j, s):
                exponent(b, par, j, s)
                p_high(b, j)
                v_high(b, par, j)

            def copy_pv(b, first=False):
                act.wait_ge(pv_done, NT * (b + 1))
                for mt in range(KT):
                    if not first:
                        act.wait_ge(out_stored[mt], DMA * b)
                    nc.scalar.activation(res[:, mt, :], pv[:, mt, :], ACT.Copy).then_inc(pv_copied, 1)

            def wx(b, mt, s, first=False):
                act.wait_ge(w_done, KT * b + mt + 1)
                if not first:
                    act.wait_ge(wx_added, KT * (b - 1) + mt + 1)
                nc.scalar.activation(wx_sb[:, mt, :], slot[s][:, :], ACT.Identity,
                                     bias=bt_sb[:, mt:mt + 1]).then_inc(wx_done, 1)

            def batch(b, par, first=False, second=False, last=False):
                tile(b, par, 0, 0)
                y_high(b, 1, first=first)
                if not first:
                    copy_pv(b - 1, first=second)
                tile(b, par, 1, 1)
                tile(b, par, 2, 0)
                tile(b, par, 3, 1)
                wx(b, 0, 0, first=first)
                tile(b, par, 4, 1)
                if not last:
                    x_high(b + 1, 1 - par)
                wx(b, 1, 0, first=first)
                tile(b, par, 5, 1)
                if not last:
                    y_high(b + 1, 0)
                exponent(b, par, 6, 0)
                p_high(b, 6)
                if not last:
                    gx_high(b + 1, 1 - par, 0, 1)
                v_high(b, par, 6)
                if not last:
                    gx_high(b + 1, 1 - par, 1, 0)
                tile(b, par, 7, 1)

            x_high(0, 0)
            y_high(0, 0, first=True)
            gx_high(0, 0, 0, 1)
            gx_high(0, 0, 1, 0)
            act.wait_ge(weights_in, 4 * DMA)
            batch(0, 0, first=True)
            batch(1, 1, second=True)
            with act.Fori(0, (B - 4) // 2) as i:
                batch(2 * i + 2, 0)
                batch(2 * i + 3, 1)
            batch(B - 2, 0)
            batch(B - 1, 1, last=True)
            copy_pv(B - 1)

        @block.vector
        def _(dve):
            setup_steps = [0]

            def setup(ins):
                setup_steps[0] += 1
                ins.then_inc(setup_dve, 1)
                dve.wait_ge(setup_dve, setup_steps[0])

            def gx_low(b, par, mt, s):
                dve.wait_ge(gx_hi_done, KT * b + mt + 1)
                nc.vector.tensor_tensor(gx_lo[par][:, mt, :], slot[s][:, :],
                                        gx_hi[par][:, mt, :].bitcast(FP32), ALU.subtract).then_inc(gx_lo_done, 1)

            def row_max(b, par, j, s):
                dve.wait_ge(e_done, NT * b + j + 1)
                nc.vector.tensor_reduce(neg_max[par][:, j:j + 1], slot[s][:, :], AX.X, ALU.max,
                                        negate=True).then_inc(max_done, 1)

            def z_copy(b, half, s):
                dve.wait_ge(z_done, 2 * b + half + 1)
                bias = bn_row[:, :].rearrange("p (a o) -> p a o", a=1).to_broadcast([P, HT, C])
                nc.vector.tensor_tensor(z_sb[:, half * HT:(half + 1) * HT, :],
                                        slot[s][:, :].rearrange("p (t o) -> p t o", t=HT), bias,
                                        ALU.add).then_inc(z_copied, 1)

            def rest(b, par, j):
                t = j % 2
                inv = row_inv[par][:, j:j + 1]
                dve.wait_ge(exp_done, NT * b + j + 1)
                nc.vector.reciprocal(inv, row_sum[par][:, j:j + 1]).then_inc(inv_done, 1)
                dve.wait_ge(p_hi_done, NT * b + j + 1)
                nc.vector.tensor_tensor(p_lo[t][:, :], p_sb[t][:, :], p_hi[t][:, :].bitcast(FP32),
                                        ALU.subtract).then_inc(p_lo_done, 1)
                dve.wait_ge(inv_done, NT * b + j + 1)
                dve.wait_ge(v_hi_done, NT * b + j + 1)
                nc.vector.scalar_tensor_tensor(out=v_lo[t][:, :], in0=z_sb[:, j, :], scalar=inv,
                                               in1=v_hi[t][:, :].bitcast(FP32), op0=ALU.mult,
                                               op1=ALU.subtract).then_inc(v_lo_done, 1)
                if j == 0:
                    nc.vector.tensor_scalar(colsum[par][:, :], p_sb[t][:, :], inv, None,
                                            ALU.mult).then_inc(acc_done, 1)
                else:
                    dve.wait_ge(acc_done, NT * b + j)
                    nc.vector.scalar_tensor_tensor(out=colsum[par][:, :], in0=p_sb[t][:, :], scalar=inv,
                                                   in1=colsum[par][:, :], op0=ALU.mult,
                                                   op1=ALU.add).then_inc(acc_done, 1)

            def col_inverse(b, s):
                dve.wait_ge(cs_done, b + 1)
                nc.vector.tensor_reduce(s_sb[:, :], slot[s][:, :].rearrange("p (t q) -> p t q", t=NT), AX.X,
                                        ALU.add).then_inc(s_read, 1)
                dve.wait_ge(s_read, b + 1)
                nc.vector.tensor_scalar(s_eps[:, :], s_sb[:, :], EPS, None, ALU.add).then_inc(s_guarded, 1)
                dve.wait_ge(s_guarded, b + 1)
                nc.vector.reciprocal(s_inv[:, :], s_eps[:, :]).then_inc(s_ready, 1)

            def scale(b, s):
                dve.wait_ge(sb_done, b + 1)
                for mt in range(KT):
                    dve.wait_ge(pv_copied, KT * b + mt + 1)
                    nc.vector.tensor_tensor(res[:, mt, :], res[:, mt, :], slot[s][:, :],
                                            ALU.mult).then_inc(scaled, 1)

            def finish(b, par):
                for mt in range(KT):
                    dve.wait_ge(wx_added, KT * b + mt + 1)
                    nc.vector.scalar_tensor_tensor(out=res[:, mt, :], in0=res[:, mt, :], scalar=0.0,
                                                   in1=x_sb[par][:, mt, :], op0=ALU.max,
                                                   op1=ALU.add).then_inc(out_ready, 1)

            def batch(b, par, first=False, last=False):
                row_max(b, par, 0, 0)
                z_copy(b, 0, 1)
                rest(b, par, 0)
                if not first:
                    col_inverse(b - 1, 0)
                row_max(b, par, 1, 1)
                z_copy(b, 1, 0)
                rest(b, par, 1)
                if not first:
                    scale(b - 1, 1)
                row_max(b, par, 2, 0)
                rest(b, par, 2)
                row_max(b, par, 3, 1)
                if not first:
                    finish(b - 1, 1 - par)
                rest(b, par, 3)
                row_max(b, par, 4, 1)
                rest(b, par, 4)
                row_max(b, par, 5, 1)
                rest(b, par, 5)
                row_max(b, par, 6, 0)
                if not last:
                    gx_low(b + 1, 1 - par, 0, 1)
                rest(b, par, 6)
                if not last:
                    gx_low(b + 1, 1 - par, 1, 0)
                row_max(b, par, 7, 1)
                rest(b, par, 7)

            dve.wait_ge(setup_mm, 1)
            g_ps = slot[0][:, 0:KT * C].rearrange("p (k c) -> p k c", k=KT)
            setup(nc.vector.tensor_copy(g_hi[:, :, :], g_ps))
            setup(nc.vector.tensor_tensor(g_lo[:, :, :], g_ps, g_hi[:, :, :].bitcast(FP32), ALU.subtract))
            dve.wait_ge(weights_in, 4 * DMA)
            setup(nc.vector.tensor_copy(wtT_hi[:, :, :], wtT_sb[:, :, :]))
            setup(nc.vector.tensor_tensor(wtT_lo[:, :, :], wtT_sb[:, :, :], wtT_hi[:, :, :].bitcast(FP32),
                                          ALU.subtract))
            dve.wait_ge(setup_mm, 2)
            h_ps = slot[1][:, 0:KT * C].rearrange("p (k c) -> p k c", k=KT)
            setup(nc.vector.tensor_scalar(hnT[:, :, :], h_ps, -1.0, None, ALU.mult))
            setup(nc.vector.tensor_scalar(bn_row[:, :], slot[1][:, BANK:BANK + C], -1.0, None, ALU.mult))
            setup(nc.vector.tensor_copy(hnT_hi[:, :, :], hnT[:, :, :]))
            setup(nc.vector.tensor_tensor(hnT_lo[:, :, :], hnT[:, :, :], hnT_hi[:, :, :].bitcast(FP32),
                                          ALU.subtract))
            gx_low(0, 0, 0, 1)
            gx_low(0, 0, 1, 0)
            run_batches(dve, lambda b: batch(b, 0, first=True), batch, lambda b: batch(b, 1, last=True))
            col_inverse(B - 1, 0)
            scale(B - 1, 1)
            finish(B - 1, 1)

        @block.tensor
        def _(pe):
            def three_passes(a_hi, a_lo, b_hi, b_lo):
                return ((a_hi, b_hi), (a_hi, b_lo), (a_lo, b_hi))

            def rows_by_n(s, lhs_hi, lhs_lo, lhs_cols, rhs_hi, rhs_lo):
                for kt in range(KT):
                    for n, (a, b) in enumerate(three_passes(lhs_hi, lhs_lo, rhs_hi, rhs_lo)):
                        for nh in range(NH):
                            cols = slice(nh * BANK, (nh + 1) * BANK)
                            last = nc.tensor.matmul(slot[s][:, cols], a[:, kt, lhs_cols], b[:, kt, cols],
                                                    start=(kt == 0 and n == 0), stop=(kt == KT - 1 and n == 2))
                return last

            def rows_of(tile):
                return slice(tile * P, (tile + 1) * P)

            def energy(b, par, j, s):
                rows_by_n(s, y_hi, y_lo, rows_of(j), gx_hi[par], gx_lo[par]).then_inc(e_done, 1)

            def z_part(b, par, half, s):
                for t in range(HT):
                    cols = slice(t * C, (t + 1) * C)
                    for kt in range(KT):
                        for n, (a, h) in enumerate(three_passes(x_hi[par], x_lo[par], hnT_hi, hnT_lo)):
                            last = nc.tensor.matmul(slot[s][:, cols], a[:, kt, rows_of(half * HT + t)], h[:, kt, :],
                                                    start=(kt == 0 and n == 0), stop=(kt == KT - 1 and n == 2))
                last.then_inc(z_done, 1)

            def w_part(b, par, mt, s):
                rows_by_n(s, wtT_hi, wtT_lo, rows_of(mt), x_hi[par], x_lo[par]).then_inc(w_done, 1)

            def g_part(b, par, mt, s):
                rows_by_n(s, g_hi, g_lo, rows_of(mt), x_hi[par], x_lo[par]).then_inc(g_done, 1)

            def pv_tile(b, j):
                pe.wait_ge(p_lo_done, NT * b + j + 1)
                pe.wait_ge(v_lo_done, NT * b + j + 1)
                t = j % 2
                for mt in range(KT):
                    for n, (v, p) in enumerate(three_passes(v_hi[t], v_lo[t], p_hi[t], p_lo[t])):
                        for nh in range(NH):
                            cols = slice(nh * BANK, (nh + 1) * BANK)
                            last = nc.tensor.matmul(pv[:, mt, cols], v[:, rows_of(mt)], p[:, cols],
                                                    start=(j == 0 and n == 0), stop=(j == NT - 1 and n == 2))
                last.then_inc(pv_done, 1)

            def turn_column_sum(b, par, s):
                pe.wait_ge(acc_done, NT * (b + 1))
                for mt in range(NT):
                    last = nc.tensor.transpose(slot[s][:, rows_of(mt)], colsum[par][:, rows_of(mt)], ident[:, :])
                last.then_inc(cs_done, 1)

            def spread(b, s):
                pe.wait_ge(s_ready, b + 1)
                for mt in range(NT):
                    last = nc.tensor.transpose(slot[s][:, rows_of(mt)], s_inv[:, mt:mt + 1].to_broadcast([P, P]),
                                               ident[:, :])
                last.then_inc(sb_done, 1)

            def batch(b, par, first=False, last=False):
                pe.wait_ge(gx_lo_done, KT * (b + 1))
                pe.wait_ge(y_lo_done, 2 * b + 1)
                energy(b, par, 0, 0)
                if not first:
                    pe.wait_ge(exp_done, NT * b)
                z_part(b, par, 0, 1)
                if not first:
                    pv_tile(b - 1, NT - 1)
                pe.wait_ge(exp_done, NT * b + 1)
                if not first:
                    turn_column_sum(b - 1, 1 - par, 0)
                pe.wait_ge(z_copied, 2 * b + 1)
                energy(b, par, 1, 1)
                if not first:
                    pe.wait_ge(s_read, b)
                z_part(b, par, 1, 0)
                if not first:
                    pe.wait_ge(pv_copied, KT * b)
                pv_tile(b, 0)
                pe.wait_ge(exp_done, NT * b + 2)
                if not first:
                    spread(b - 1, 1)
                pe.wait_ge(z_copied, 2 * b + 2)
                energy(b, par, 2, 0)
                pv_tile(b, 1)
                if not first:
                    pe.wait_ge(scaled, KT * b)
                energy(b, par, 3, 1)
                pe.wait_ge(exp_done, NT * b + 3)
                w_part(b, par, 0, 0)
                pv_tile(b, 2)
                pe.wait_ge(exp_done, NT * b + 4)
                pe.wait_ge(y_lo_done, 2 * b + 2)
                energy(b, par, 4, 1)
                pe.wait_ge(wx_done, KT * b + 1)
                w_part(b, par, 1, 0)
                pv_tile(b, 3)
                pe.wait_ge(exp_done, NT * b + 5)
                energy(b, par, 5, 1)
                pv_tile(b, 4)
                pe.wait_ge(wx_done, KT * b + 2)
                energy(b, par, 6, 0)
                pe.wait_ge(exp_done, NT * b + 6)
                if not last:
                    pe.wait_ge(x_lo_done, KT * (b + 2))
                    g_part(b + 1, 1 - par, 0, 1)
                pv_tile(b, 5)
                if not last:
                    pe.wait_ge(exp_done, NT * b + 7)
                    g_part(b + 1, 1 - par, 1, 0)
                    pe.wait_ge(gx_lo_done, KT * (b + 1) + 1)
                energy(b, par, 7, 1)
                pv_tile(b, 6)

            pe.wait_ge(wqk_in, DMA)
            for ct in range(KT):
                for kt in range(KT):
                    last = nc.tensor.matmul(slot[0][:, ct * C:(ct + 1) * C], wqk_sb[:, kt, rows_of(ct)],
                                            wqk_sb[:, kt, :], start=(kt == 0), stop=(kt == KT - 1))
            last.then_inc(setup_mm, 1)
            pe.wait_ge(weights_in, 4 * DMA)
            for ct in range(KT):
                for kt in range(KT):
                    nc.tensor.matmul(slot[1][:, ct * C:(ct + 1) * C], wv_sb[:, kt, rows_of(ct)], wtT_sb[:, kt, :],
                                     start=(kt == 0), stop=(kt == KT - 1))
            for kt in range(KT):
                last = nc.tensor.matmul(slot[1][:, BANK:BANK + C], bv_sb[:, kt:kt + 1].to_broadcast([P, P]),
                                        wtT_sb[:, kt, :], start=(kt == 0), stop=(kt == KT - 1))
            last.then_inc(setup_mm, 1)
            pe.wait_ge(setup_dve, 8)
            pe.wait_ge(ident_made, 2)
            pe.wait_ge(x_lo_done, KT)
            g_part(0, 0, 0, 1)
            g_part(0, 0, 1, 0)
            run_batches(pe, lambda b: batch(b, 0, first=True), batch, lambda b: batch(b, 1, last=True))
            pv_tile(B - 1, NT - 1)
            turn_column_sum(B - 1, 1, 0)
            pe.wait_ge(exp_done, NT * B)
            spread(B - 1, 1)


def kernel(x, ctx_2048, L0_xattn_w_qk, L0_xattn_w_v, L0_xattn_b_v, L0_xattn_w_t, L0_xattn_b_t):
    import numpy as np
    import concourse.bacc as bacc
    from concourse.bass_utils import run_bass_kernel_spmd

    nc = bacc.Bacc("TRN2", target_bir_lowering=False, num_devices=1)
    given = {
        "x": x, "y": ctx_2048, "w_qk": L0_xattn_w_qk, "w_v": L0_xattn_w_v, "b_v": L0_xattn_b_v,
        "w_t_T": np.asarray(L0_xattn_w_t).T, "b_t": L0_xattn_b_t,
    }
    arrays, aps = {}, []
    for name, value in given.items():
        a = np.ascontiguousarray(value)
        arrays[name] = a
        aps.append(nc.dram_tensor(name, a.shape, mybir.dt.from_np(a.dtype), kind="ExternalInput").ap())
    aps.append(nc.dram_tensor("out", arrays["x"].shape, FP32, kind="ExternalOutput").ap())
    xattn_kernel(nc, *aps)
    result = run_bass_kernel_spmd(nc, [arrays], core_ids=[0])
    return result.results[0]["out"]
```

```python
import concourse.bass as bass
from concourse import mybir
from contextlib import ExitStack

FP32 = mybir.dt.float32
FP32R = mybir.dt.float32r
ALU = mybir.AluOpType
ACT = mybir.ActivationFunctionType
AX = mybir.AxisListType

P = 128
Q = 32
BANK = 512
EPS = 1e-07


def xattn_kernel(nc: bass.Bass, x: bass.AP, y: bass.AP, w_qk: bass.AP, w_v: bass.AP, b_v: bass.AP,
                 w_t_T: bass.AP, b_t: bass.AP, out: bass.AP):
    B, C, N = x.shape
    KT = C // P
    NT = N // P
    NH = N // BANK
    HT = NT // 2
    HN = N // 2
    DMA = 16

    def by_channel(ap):
        return ap.rearrange("(k p) n -> p k n", p=P)

    x_dram = x.rearrange("b (k p) n -> b p k n", p=P)
    y_dram = y.rearrange("b (k p) n -> b p k n", p=P)
    out_dram = out.rearrange("b (k p) n -> b p k n", p=P)

    ctx = ExitStack()
    with ctx:
        def sb(name, shape, dt=FP32):
            return ctx.enter_context(nc.sbuf_tensor(name, shape, dt))

        def sem(name):
            return ctx.enter_context(nc.semaphore(name))

        wqk_sb = sb("wqk_sb", [P, KT, C])
        wv_sb = sb("wv_sb", [P, KT, C])
        wtT_sb = sb("wtT_sb", [P, KT, C])
        bv_sb = sb("bv_sb", [P, KT])
        bt_sb = sb("bt_sb", [P, KT])
        g_hi, g_lo = sb("g_hi", [P, KT, C], FP32R), sb("g_lo", [P, KT, C], FP32R)
        hnT = sb("hnT", [P, KT, C])
        hnT_hi, hnT_lo = sb("hnT_hi", [P, KT, C], FP32R), sb("hnT_lo", [P, KT, C], FP32R)
        wtT_hi, wtT_lo = sb("wtT_hi", [P, KT, C], FP32R), sb("wtT_lo", [P, KT, C], FP32R)
        eps_wb, bias = sb("eps_wb", [P, KT]), sb("bias", [P, KT])
        same_row = sb("same_row", [P, P])
        x_sb = [sb(f"x_sb{i}", [P, KT, N]) for i in range(2)]
        x_hi = [sb(f"x_hi{i}", [P, KT, N], FP32R) for i in range(2)]
        x_lo = [sb(f"x_lo{i}", [P, KT, N], FP32R) for i in range(2)]
        gx_hi = [sb(f"gx_hi{i}", [P, KT, N], FP32R) for i in range(2)]
        gx_lo = [sb(f"gx_lo{i}", [P, KT, N], FP32R) for i in range(2)]
        y_sb = sb("y_sb", [P, KT, N])
        y_hi, y_lo = sb("y_hi", [P, KT, N], FP32R), sb("y_lo", [P, KT, N], FP32R)
        z_sb = sb("z_sb", [P, NT, C])
        res = sb("res", [P, KT, N])
        colsum = [sb(f"colsum{i}", [P, N]) for i in range(2)]
        colsum_T = sb("colsum_T", [P, N // Q, Q])
        s_part, s_eps, s_inv = (sb(name, [P, N // Q]) for name in ("s_part", "s_eps", "s_inv"))
        s_inv_all = sb("s_inv_all", [P, N])
        neg_max = [sb(f"neg_max{i}", [P, NT]) for i in range(2)]
        row_sum = [sb(f"row_sum{i}", [P, NT]) for i in range(2)]
        row_inv = [sb(f"row_inv{i}", [P, NT]) for i in range(2)]
        p_sb = [sb(f"p_sb{i}", [P, N]) for i in range(2)]
        p_hi = [sb(f"p_hi{i}", [P, N], FP32R) for i in range(2)]
        p_lo = [sb(f"p_lo{i}", [P, N], FP32R) for i in range(2)]
        v_hi = [sb(f"v_hi{i}", [P, C], FP32R) for i in range(2)]
        v_lo = [sb(f"v_lo{i}", [P, C], FP32R) for i in range(2)]
        pv = ctx.enter_context(nc.psum_tensor("pv", [P, KT, N], FP32))
        slot = [ctx.enter_context(nc.psum_tensor(f"slot{i}", [P, N], FP32)) for i in range(2)]

        wqk_in, weights_in, y_in = sem("wqk_in"), sem("weights_in"), sem("y_in")
        x_in = [sem(f"x_in{kt}") for kt in range(KT)]
        out_stored = [sem(f"out_stored{mt}") for mt in range(KT)]
        same_row_made = sem("same_row_made")
        setup_mm, setup_dve = sem("setup_mm"), sem("setup_dve")
        e_done, pv_done, z_done = sem("e_done"), sem("pv_done"), sem("z_done")
        w_done, g_done = sem("w_done"), sem("g_done")
        s_done = sem("s_done")
        exp_done, p_hi_done, v_hi_done = sem("exp_done"), sem("p_hi_done"), sem("v_hi_done")
        x_hi_done, y_hi_done, gx_hi_done = sem("x_hi_done"), sem("y_hi_done"), sem("gx_hi_done")
        pv_copied, z_copied = sem("pv_copied"), sem("z_copied")
        max_done, inv_done = sem("max_done"), sem("inv_done")
        p_lo_done, v_lo_done, acc_done = sem("p_lo_done"), sem("v_lo_done"), sem("acc_done")
        gx_lo_done = sem("gx_lo_done")
        turned, s_parted, s_guarded = sem("turned"), sem("s_parted"), sem("s_guarded")
        s_inverted, s_spread = sem("s_inverted"), sem("s_spread")
        scaled, wx_added, out_ready = sem("scaled"), sem("wx_added"), sem("out_ready")
        x_lo_done, y_lo_done = sem("x_lo_done"), sem("y_lo_done")

        block = ctx.enter_context(nc.Block())

        def run_batches(eng, first, middle, last):
            first(0)
            with eng.Fori(0, (B - 2) // 2) as i:
                middle(2 * i + 1, 1)
                middle(2 * i + 2, 0)
            last(B - 1)

        @block.sync
        def _(sp):
            def load_x(b, par, kt):
                sp.dma_start(x_sb[par][:, kt, :], x_dram[b][:, kt, :]).then_inc(x_in[kt], DMA)

            def load_y(b):
                sp.dma_start(y_sb[:, :, :], y_dram[b]).then_inc(y_in, DMA)

            def store(b, mt):
                sp.wait_ge(out_ready, KT * b + mt + 1)
                sp.dma_start(out_dram[b][:, mt, :], res[:, mt, :]).then_inc(out_stored[mt], DMA)

            def batch(b, par, first=False, last=False):
                if not last:
                    sp.wait_ge(y_hi_done, 2 * b + 2)
                    sp.wait_ge(y_lo_done, 2 * b + 2)
                    load_y(b + 1)
                for t in range(KT):
                    if not first:
                        store(b - 1, t)
                    if not last:
                        load_x(b + 1, 1 - par, t)

            sp.dma_start(wqk_sb[:, :, :], by_channel(w_qk)).then_inc(wqk_in, DMA)
            sp.dma_start(wtT_sb[:, :, :], by_channel(w_t_T)).then_inc(weights_in, DMA)
            sp.dma_start(wv_sb[:, :, :], by_channel(w_v)).then_inc(weights_in, DMA)
            for kt in range(KT):
                load_x(0, 0, kt)
            load_y(0)
            run_batches(sp, lambda b: batch(b, 0, first=True), batch, lambda b: batch(b, 1, last=True))
            for mt in range(KT):
                store(B - 1, mt)
            for mt in range(KT):
                sp.wait_ge(out_stored[mt], DMA * B)

        @block.gpsimd
        def _(pool):
            def x_low(b, par, kt):
                pool.wait_ge(x_hi_done, KT * b + kt + 1)
                nc.gpsimd.tensor_tensor(x_lo[par][:, kt, :], x_sb[par][:, kt, :],
                                        x_hi[par][:, kt, :].bitcast(FP32), ALU.subtract).then_inc(x_lo_done, 1)

            def y_low(b, half):
                cols = slice(half * HN, (half + 1) * HN)
                pool.wait_ge(y_hi_done, 2 * b + half + 1)
                nc.gpsimd.tensor_tensor(y_lo[:, :, cols], y_sb[:, :, cols],
                                        y_hi[:, :, cols].bitcast(FP32), ALU.subtract).then_inc(y_lo_done, 1)

            def batch(b, par, first=False, last=False):
                y_low(b, 1)
                if not last:
                    for kt in range(KT):
                        x_low(b + 1, 1 - par, kt)
                    y_low(b + 1, 0)

            nc.gpsimd.memset(same_row[:, :], 0.0).then_inc(same_row_made, 1)
            for q in range(P // Q):
                pool.wait_ge(same_row_made, q + 1)
                by_quadrant = same_row[:, :].rearrange("p (g i) -> p g i", i=Q)
                nc.gpsimd.affine_select(out=by_quadrant, in_=by_quadrant, compare_op=ALU.not_equal, fill=1.0,
                                        base=-Q * q, pattern=[[0, P // Q], [-1, Q]],
                                        channel_multiplier=1).then_inc(same_row_made, 1)
            x_low(0, 0, 0)
            y_low(0, 0)
            run_batches(pool, lambda b: batch(b, 0, first=True), batch, lambda b: batch(b, 1, last=True))

        @block.scalar
        def _(act):
            def x_high(b, par, kt, early=False):
                act.wait_ge(x_in[kt], DMA * (b + 1))
                if not early:
                    act.wait_ge(w_done, KT * (b - 1))
                nc.scalar.activation(x_hi[par][:, kt, :], x_sb[par][:, kt, :], ACT.Copy).then_inc(x_hi_done, 1)

            def y_high(b, half, first=False):
                cols = slice(half * HN, (half + 1) * HN)
                act.wait_ge(y_in, DMA * (b + 1))
                if not first:
                    act.wait_ge(e_done, NT * (b - 1) + HT * (half + 1))
                nc.scalar.activation(y_hi[:, :, cols], y_sb[:, :, cols], ACT.Copy).then_inc(y_hi_done, 1)

            def gx_high(b, par, mt, s):
                act.wait_ge(g_done, KT * b + mt + 1)
                nc.scalar.activation(gx_hi[par][:, mt, :], slot[s][:, :], ACT.Copy).then_inc(gx_hi_done, 1)

            def exponent(b, par, j, s):
                act.wait_ge(max_done, NT * b + j + 1)
                if j >= 2 or not isinstance(b, int) or b > 0:
                    act.wait_ge(acc_done, NT * b + j - 1)
                nc.scalar.activation(p_sb[j % 2][:, :], slot[s][:, :], ACT.Exp, bias=neg_max[par][:, j:j + 1],
                                     accum_out=row_sum[par][:, j:j + 1]).then_inc(exp_done, 1)

            def p_high(b, j):
                act.wait_ge(exp_done, NT * b + j + 1)
                if j >= 2 or not isinstance(b, int) or b > 0:
                    act.wait_ge(pv_done, NT * b + j - 1)
                nc.scalar.activation(p_hi[j % 2][:, :], p_sb[j % 2][:, :], ACT.Copy).then_inc(p_hi_done, 1)

            def z_copy(b, half, s, first=False):
                act.wait_ge(z_done, 2 * b + half + 1)
                if not first:
                    act.wait_ge(v_lo_done, NT * (b - 1) + HT * (half + 1))
                nc.scalar.activation(z_sb[:, half * HT:(half + 1) * HT, :],
                                     slot[s][:, :].rearrange("p (t o) -> p t o", t=HT),
                                     ACT.Copy).then_inc(z_copied, 1)

            def v_high(b, par, j):
                if j % HT == 0:
                    act.wait_ge(z_copied, 2 * b + j // HT + 1)
                act.wait_ge(inv_done, NT * b + j + 1)
                nc.scalar.activation(v_hi[j % 2][:, :], z_sb[:, j, :], ACT.Copy,
                                     scale=row_inv[par][:, j:j + 1]).then_inc(v_hi_done, 1)

            def tile(b, par, j, s):
                exponent(b, par, j, s)
                p_high(b, j)
                v_high(b, par, j)

            def copy_pv(b, first=False):
                act.wait_ge(pv_done, NT * (b + 1))
                for mt in range(KT):
                    if not first:
                        act.wait_ge(out_stored[mt], DMA * b)
                    nc.scalar.activation(res[:, mt, :], pv[:, mt, :], ACT.Copy).then_inc(pv_copied, 1)

            def batch(b, par, first=False, second=False, last=False):
                own, other = par, 1 - par
                if first:
                    z_copy(b, 0, other, first=first)
                exponent(b, par, 0, own)
                if not first:
                    z_copy(b, 0, other)
                p_high(b, 0)
                v_high(b, par, 0)
                if not first:
                    copy_pv(b - 1, first=second)
                y_high(b, 1, first=first)
                exponent(b, par, 1, other)
                p_high(b, 1)
                z_copy(b, 1, own, first=first)
                v_high(b, par, 1)
                tile(b, par, 2, other)
                tile(b, par, 3, other if not first else own)
                if not last:
                    x_high(b + 1, 1 - par, 0, early=first)
                tile(b, par, 4, other)
                if not last:
                    x_high(b + 1, 1 - par, 1, early=first)
                tile(b, par, 5, own)
                if not last:
                    y_high(b + 1, 0)
                exponent(b, par, 6, other)
                p_high(b, 6)
                if not last:
                    gx_high(b + 1, 1 - par, 0, own)
                v_high(b, par, 6)
                if not last:
                    gx_high(b + 1, 1 - par, 1, other)
                tile(b, par, 7, own)

            with nc.allow_non_contiguous_dma(reason="256 biases, once"):
                act.dma_start(bv_sb[:, :], b_v.rearrange("(k p) -> p k", p=P)).then_inc(weights_in, DMA)
                act.dma_start(bt_sb[:, :], b_t.rearrange("(k p) -> p k", p=P)).then_inc(weights_in, DMA)
            for kt in range(KT):
                x_high(0, 0, kt, early=True)
            y_high(0, 0, first=True)
            gx_high(0, 0, 0, 1)
            gx_high(0, 0, 1, 0)
            batch(0, 0, first=True)
            batch(1, 1, second=True)
            with act.Fori(0, (B - 4) // 2) as i:
                batch(2 * i + 2, 0)
                batch(2 * i + 3, 1)
            batch(B - 2, 0)
            batch(B - 1, 1, last=True)
            copy_pv(B - 1)

        @block.vector
        def _(dve):
            setup_steps = [0]

            def setup(ins):
                setup_steps[0] += 1
                ins.then_inc(setup_dve, 1)
                dve.wait_ge(setup_dve, setup_steps[0])

            def gx_low(b, par, mt, s):
                dve.wait_ge(gx_hi_done, KT * b + mt + 1)
                nc.vector.tensor_tensor(gx_lo[par][:, mt, :], slot[s][:, :],
                                        gx_hi[par][:, mt, :].bitcast(FP32), ALU.subtract).then_inc(gx_lo_done, 1)

            def row_max(b, par, j, s):
                dve.wait_ge(e_done, NT * b + j + 1)
                nc.vector.tensor_reduce(neg_max[par][:, j:j + 1], slot[s][:, :], AX.X, ALU.max,
                                        negate=True).then_inc(max_done, 1)

            def row_inverse(b, par, j):
                dve.wait_ge(exp_done, NT * b + j + 1)
                nc.vector.reciprocal(row_inv[par][:, j:j + 1], row_sum[par][:, j:j + 1]).then_inc(inv_done, 1)

            def p_low(b, j):
                t = j % 2
                dve.wait_ge(p_hi_done, NT * b + j + 1)
                nc.vector.tensor_tensor(p_lo[t][:, :], p_sb[t][:, :], p_hi[t][:, :].bitcast(FP32),
                                        ALU.subtract).then_inc(p_lo_done, 1)

            def v_low(b, par, j):
                t = j % 2
                dve.wait_ge(v_hi_done, NT * b + j + 1)
                nc.vector.scalar_tensor_tensor(out=v_lo[t][:, :], in0=z_sb[:, j, :],
                                               scalar=row_inv[par][:, j:j + 1],
                                               in1=v_hi[t][:, :].bitcast(FP32), op0=ALU.mult,
                                               op1=ALU.subtract).then_inc(v_lo_done, 1)

            def column_sum(b, par, j):
                inv = row_inv[par][:, j:j + 1]
                dve.wait_ge(inv_done, NT * b + j + 1)
                if j == 0:
                    nc.vector.tensor_scalar(colsum[par][:, :], p_sb[j % 2][:, :], inv, None,
                                            ALU.mult).then_inc(acc_done, 1)
                else:
                    dve.wait_ge(acc_done, NT * b + j)
                    nc.vector.scalar_tensor_tensor(out=colsum[par][:, :], in0=p_sb[j % 2][:, :], scalar=inv,
                                                   in1=colsum[par][:, :], op0=ALU.mult,
                                                   op1=ALU.add).then_inc(acc_done, 1)

            def turn(b, par):
                dve.wait_ge(acc_done, NT * (b + 1))
                nc.vector.transpose(colsum_T[:, :, :],
                                    colsum[par][:, :].rearrange("p (t q) -> p t q", q=Q)).then_inc(turned, 1)

            def part_sum(b):
                dve.wait_ge(turned, b + 1)
                nc.vector.tensor_reduce(s_part[:, :], colsum_T[:, :, :], AX.X, ALU.add).then_inc(s_parted, 1)

            def col_inverse(b, s):
                dve.wait_ge(s_done, b + 1)
                nc.vector.tensor_scalar(s_eps[:, :], slot[s][:, 0:N // Q], EPS, None,
                                        ALU.add).then_inc(s_guarded, 1)
                dve.wait_ge(s_guarded, b + 1)
                nc.vector.reciprocal(s_inv[:, :], s_eps[:, :]).then_inc(s_inverted, 1)
                dve.wait_ge(s_inverted, b + 1)
                nc.vector.transpose(s_inv_all[:, :].rearrange("p (t q) -> p t q", q=Q),
                                    s_inv[:, :].rearrange("p (t a) -> p t a", a=1)
                                    .to_broadcast([P, N // Q, Q])).then_inc(s_spread, 1)

            def scale(b, mt):
                dve.wait_ge(s_spread, b + 1)
                dve.wait_ge(pv_copied, KT * b + mt + 1)
                nc.vector.scalar_tensor_tensor(out=res[:, mt, :], in0=res[:, mt, :],
                                               scalar=eps_wb[:, mt:mt + 1], in1=s_inv_all[:, :],
                                               op0=ALU.add, op1=ALU.mult).then_inc(scaled, 1)

            def add_wx(b, mt, wx):
                dve.wait_ge(w_done, KT * b + mt + 1)
                dve.wait_ge(scaled, KT * b + mt + 1)
                nc.vector.scalar_tensor_tensor(out=res[:, mt, :], in0=wx, scalar=bias[:, mt:mt + 1],
                                               in1=res[:, mt, :], op0=ALU.add, op1=ALU.add).then_inc(wx_added, 1)

            def finish(b, par, mt):
                dve.wait_ge(wx_added, KT * b + mt + 1)
                nc.vector.scalar_tensor_tensor(out=res[:, mt, :], in0=res[:, mt, :], scalar=0.0,
                                               in1=x_sb[par][:, mt, :], op0=ALU.max,
                                               op1=ALU.add).then_inc(out_ready, 1)

            def tile(b, par, j, s):
                row_max(b, par, j, s)
                if j > 0:
                    column_sum(b, par, j - 1)
                row_inverse(b, par, j)

            def low_parts(b, par, j):
                p_low(b, j)
                v_low(b, par, j)

            def batch(b, par, first=False, last=False):
                own, other = par, 1 - par
                row_max(b, par, 0, own)
                if not first:
                    turn(b - 1, 1 - par)
                row_inverse(b, par, 0)
                if not first:
                    part_sum(b - 1)
                low_parts(b, par, 0)
                if not first:
                    col_inverse(b - 1, own)
                tile(b, par, 1, other)
                if not first:
                    scale(b - 1, 0)
                low_parts(b, par, 1)
                if not first:
                    scale(b - 1, 1)
                tile(b, par, 2, other)
                if not first:
                    add_wx(b - 1, 0, slot[own][:, :])
                low_parts(b, par, 2)
                if not first:
                    finish(b - 1, 1 - par, 0)
                tile(b, par, 3, other if not first else own)
                if not first:
                    add_wx(b - 1, 1, slot[own][:, :])
                low_parts(b, par, 3)
                if not first:
                    finish(b - 1, 1 - par, 1)
                tile(b, par, 4, other)
                low_parts(b, par, 4)
                tile(b, par, 5, own)
                low_parts(b, par, 5)
                tile(b, par, 6, other)
                p_low(b, 6)
                if not last:
                    gx_low(b + 1, 1 - par, 0, own)
                v_low(b, par, 6)
                if not last:
                    gx_low(b + 1, 1 - par, 1, other)
                tile(b, par, 7, own)
                low_parts(b, par, 7)
                column_sum(b, par, 7)

            dve.wait_ge(setup_mm, 1)
            g_ps = slot[0][:, 0:KT * C].rearrange("p (k c) -> p k c", k=KT)
            setup(nc.vector.tensor_copy(g_hi[:, :, :], g_ps))
            setup(nc.vector.tensor_tensor(g_lo[:, :, :], g_ps, g_hi[:, :, :].bitcast(FP32), ALU.subtract))
            dve.wait_ge(x_hi_done, KT)
            nc.vector.tensor_tensor(x_lo[0][:, KT - 1, :], x_sb[0][:, KT - 1, :],
                                    x_hi[0][:, KT - 1, :].bitcast(FP32), ALU.subtract).then_inc(x_lo_done, 1)
            dve.wait_ge(setup_mm, 2)
            h_ps = pv[:, 0, 0:KT * C].rearrange("p (k c) -> p k c", k=KT)
            wb_ps = pv[:, 1, 0:KT]
            setup(nc.vector.tensor_scalar(hnT[:, :, :], h_ps, -1.0, None, ALU.mult))
            setup(nc.vector.tensor_copy(hnT_hi[:, :, :], hnT[:, :, :]))
            setup(nc.vector.tensor_tensor(hnT_lo[:, :, :], hnT[:, :, :], hnT_hi[:, :, :].bitcast(FP32),
                                          ALU.subtract))
            setup(nc.vector.tensor_scalar(eps_wb[:, :], wb_ps, EPS, None, ALU.mult))
            dve.wait_ge(weights_in, 4 * DMA)
            setup(nc.vector.tensor_tensor(bias[:, :], bt_sb[:, :], wb_ps, ALU.subtract))
            gx_low(0, 0, 0, 1)
            gx_low(0, 0, 1, 0)
            setup(nc.vector.tensor_copy(wtT_hi[:, :, :], wtT_sb[:, :, :]))
            setup(nc.vector.tensor_tensor(wtT_lo[:, :, :], wtT_sb[:, :, :], wtT_hi[:, :, :].bitcast(FP32),
                                          ALU.subtract))
            run_batches(dve, lambda b: batch(b, 0, first=True), batch, lambda b: batch(b, 1, last=True))
            turn(B - 1, 1)
            part_sum(B - 1)
            col_inverse(B - 1, 1)
            scale(B - 1, 0)
            scale(B - 1, 1)
            add_wx(B - 1, 0, slot[0][:, :])
            finish(B - 1, 1, 0)
            add_wx(B - 1, 1, pv[:, 0, :])
            finish(B - 1, 1, 1)

        @block.tensor
        def _(pe):
            def three_passes(a_hi, a_lo, b_hi, b_lo):
                return ((a_hi, b_hi), (a_hi, b_lo), (a_lo, b_hi))

            def rows_by_n(dst, lhs_hi, lhs_lo, lhs_cols, rhs_hi, rhs_lo):
                for kt in range(KT):
                    for n, (a, b) in enumerate(three_passes(lhs_hi, lhs_lo, rhs_hi, rhs_lo)):
                        for nh in range(NH):
                            cols = slice(nh * BANK, (nh + 1) * BANK)
                            last = nc.tensor.matmul(dst[:, cols], a[:, kt, lhs_cols], b[:, kt, cols],
                                                    start=(kt == 0 and n == 0), stop=(kt == KT - 1 and n == 2))
                return last

            def rows_of(tile):
                return slice(tile * P, (tile + 1) * P)

            def energy(b, par, j, s):
                rows_by_n(slot[s][:, :], y_hi, y_lo, rows_of(j), gx_hi[par], gx_lo[par]).then_inc(e_done, 1)

            def z_part(b, par, half, s):
                for t in range(HT):
                    cols = slice(t * C, (t + 1) * C)
                    for kt in range(KT):
                        for n, (a, h) in enumerate(three_passes(x_hi[par], x_lo[par], hnT_hi, hnT_lo)):
                            last = nc.tensor.matmul(slot[s][:, cols], a[:, kt, rows_of(half * HT + t)], h[:, kt, :],
                                                    start=(kt == 0 and n == 0), stop=(kt == KT - 1 and n == 2))
                last.then_inc(z_done, 1)

            def w_part(b, par, mt, dst):
                rows_by_n(dst, wtT_hi, wtT_lo, rows_of(mt), x_hi[par], x_lo[par]).then_inc(w_done, 1)

            def g_part(b, par, mt, s):
                rows_by_n(slot[s][:, :], g_hi, g_lo, rows_of(mt), x_hi[par], x_lo[par]).then_inc(g_done, 1)

            def pv_tile(b, j):
                t = j % 2
                passes = ((v_hi[t], p_hi[t], v_hi_done),
                          (v_lo[t], p_hi[t], v_lo_done),
                          (v_hi[t], p_lo[t], p_lo_done))
                for n, (v, p, ready) in enumerate(passes):
                    pe.wait_ge(ready, NT * b + j + 1)
                    for mt in range(KT):
                        for nh in range(NH):
                            cols = slice(nh * BANK, (nh + 1) * BANK)
                            last = nc.tensor.matmul(pv[:, mt, cols], v[:, rows_of(mt)], p[:, cols],
                                                    start=(j == 0 and n == 0), stop=(j == NT - 1 and n == 2))
                last.then_inc(pv_done, 1)

            def add_quadrants(b, s):
                pe.wait_ge(s_parted, b + 1)
                nc.tensor.matmul(slot[s][:, 0:N // Q], same_row[:, :], s_part[:, :],
                                 start=True, stop=True).then_inc(s_done, 1)

            def batch(b, par, first=False, last=False):
                own, other = par, 1 - par
                if first:
                    pe.wait_ge(setup_dve, 5)
                    pe.wait_ge(gx_lo_done, 1)
                    z_part(b, par, 0, other)
                pe.wait_ge(gx_lo_done, KT * (b + 1))
                pe.wait_ge(y_lo_done, 2 * b + 1)
                energy(b, par, 0, own)
                if not first:
                    pe.wait_ge(exp_done, NT * b)
                    z_part(b, par, 0, other)
                    pv_tile(b - 1, NT - 1)
                    pe.wait_ge(exp_done, NT * b + 1)
                    add_quadrants(b - 1, own)
                pe.wait_ge(z_copied, 2 * b + 1)
                energy(b, par, 1, other)
                if first:
                    pe.wait_ge(exp_done, NT * b + 1)
                else:
                    pe.wait_ge(s_guarded, b)
                z_part(b, par, 1, own)
                if first:
                    pe.wait_ge(setup_dve, 7)
                else:
                    pe.wait_ge(pv_copied, KT * b)
                pv_tile(b, 0)
                pe.wait_ge(exp_done, NT * b + 2)
                energy(b, par, 2, other)
                pe.wait_ge(z_copied, 2 * b + 2)
                if not first:
                    w_part(b - 1, 1 - par, 0, slot[own][:, :])
                pv_tile(b, 1)
                if first:
                    energy(b, par, 3, own)
                else:
                    pe.wait_ge(exp_done, NT * b + 3)
                    energy(b, par, 3, other)
                    pe.wait_ge(wx_added, KT * (b - 1) + 1)
                    w_part(b - 1, 1 - par, 1, slot[own][:, :])
                pv_tile(b, 2)
                pe.wait_ge(exp_done, NT * b + 4)
                pe.wait_ge(y_lo_done, 2 * b + 2)
                energy(b, par, 4, other)
                pv_tile(b, 3)
                if not first:
                    pe.wait_ge(wx_added, KT * b)
                energy(b, par, 5, own)
                pv_tile(b, 4)
                pe.wait_ge(exp_done, NT * b + 5)
                energy(b, par, 6, other)
                pe.wait_ge(exp_done, NT * b + 6)
                if not last:
                    pe.wait_ge(x_lo_done, KT * (b + 2))
                    g_part(b + 1, 1 - par, 0, own)
                pv_tile(b, 5)
                if not last:
                    pe.wait_ge(exp_done, NT * b + 7)
                    g_part(b + 1, 1 - par, 1, other)
                    pe.wait_ge(gx_lo_done, KT * (b + 1) + 1)
                energy(b, par, 7, own)
                pv_tile(b, 6)

            pe.wait_ge(wqk_in, DMA)
            for ct in range(KT):
                for kt in range(KT):
                    last = nc.tensor.matmul(slot[0][:, ct * C:(ct + 1) * C], wqk_sb[:, kt, rows_of(ct)],
                                            wqk_sb[:, kt, :], start=(kt == 0), stop=(kt == KT - 1))
            last.then_inc(setup_mm, 1)
            pe.wait_ge(weights_in, 4 * DMA)
            for ct in range(KT):
                for kt in range(KT):
                    nc.tensor.matmul(pv[:, 0, ct * C:(ct + 1) * C], wv_sb[:, kt, rows_of(ct)], wtT_sb[:, kt, :],
                                     start=(kt == 0), stop=(kt == KT - 1))
            for mt in range(KT):
                for kt in range(KT):
                    last = nc.tensor.matmul(pv[:, 1, mt:mt + 1], wtT_sb[:, kt, rows_of(mt)], bv_sb[:, kt:kt + 1],
                                            start=(kt == 0), stop=(kt == KT - 1))
            last.then_inc(setup_mm, 1)
            pe.wait_ge(setup_dve, 2)
            pe.wait_ge(x_lo_done, KT)
            g_part(0, 0, 0, 1)
            g_part(0, 0, 1, 0)
            pe.wait_ge(same_row_made, P // Q + 1)
            run_batches(pe, lambda b: batch(b, 0, first=True), batch, lambda b: batch(b, 1, last=True))
            pe.wait_ge(exp_done, NT * B - 1)
            w_part(B - 1, 1, 0, slot[0][:, :])
            pv_tile(B - 1, NT - 1)
            pe.wait_ge(exp_done, NT * B)
            add_quadrants(B - 1, 1)
            pe.wait_ge(pv_copied, KT * (B - 1) + 1)
            w_part(B - 1, 1, 1, pv[:, 0, :])


def kernel(x, ctx_2048, L0_xattn_w_qk, L0_xattn_w_v, L0_xattn_b_v, L0_xattn_w_t, L0_xattn_b_t):
    import numpy as np
    import concourse.bacc as bacc
    from concourse.bass_utils import run_bass_kernel_spmd

    nc = bacc.Bacc("TRN2", target_bir_lowering=False, num_devices=1)
    given = {
        "x": x, "y": ctx_2048, "w_qk": L0_xattn_w_qk, "w_v": L0_xattn_w_v, "b_v": L0_xattn_b_v,
        "w_t_T": np.asarray(L0_xattn_w_t).T, "b_t": L0_xattn_b_t,
    }
    arrays, aps = {}, []
    for name, value in given.items():
        a = np.ascontiguousarray(value)
        arrays[name] = a
        aps.append(nc.dram_tensor(name, a.shape, mybir.dt.from_np(a.dtype), kind="ExternalInput").ap())
    aps.append(nc.dram_tensor("out", arrays["x"].shape, FP32, kind="ExternalOutput").ap())
    xattn_kernel(nc, *aps)
    result = run_bass_kernel_spmd(nc, [arrays], core_ids=[0])
    return result.results[0]["out"]
```
